# Optimizing a Trainium2 kernel written in Bass

```python
import numpy as np
import jax
import jax.numpy as jnp

def _softmax(x, axis=-1):
    return jax.nn.softmax(x, axis=axis)

def _gelu(x):
    return jax.nn.gelu(x, approximate=True)

def _silu(x):
    return jax.nn.silu(x)

def _sigmoid(x):
    return jax.nn.sigmoid(x)

def _layernorm(x, axis=-1, eps=1e-05):
    m = jnp.mean(x, axis=axis, keepdims=True)
    v = jnp.var(x, axis=axis, keepdims=True)
    return (x - m) / jnp.sqrt(v + eps)

def _scatter_add(tgt, idx, src, axis=0):
    return tgt.at[idx].add(src)

def _segment_sum(src, seg, n):
    return jax.ops.segment_sum(src, seg, n)
kernel_name = 'mk_adj_preln_d1_adj_r2_86a46e'

def setup_inputs(seed: int=0):
    np.random.seed(seed)
    _w = jnp.asarray

    def _rec_inputs():
        import jax
        import jax.numpy as jnp
        _gk = jax.random.key(seed)
        x = 0.0001732 + 1 * jax.random.normal(jax.random.fold_in(_gk, 1), (5120, 64), jnp.float32)
        _a = jax.random.bernoulli(jax.random.fold_in(_gk, 2), 0.0015625, (5120, 5120))
        _a = jnp.logical_or(_a, jnp.swapaxes(_a, -1, -2))
        _a = jnp.logical_or(_a, jnp.eye(5120, dtype=bool))
        _af = _a.astype(jnp.float32)
        _af = _af * jax.random.uniform(jax.random.fold_in(_gk, 3), (5120, 5120), jnp.float32, 0.05, 0.02)
        adj = _af
        return (x, adj)
    x, adj = _rec_inputs()

    def _L0_gnn_setup():
        import jax, jax.numpy as jnp
        import numpy as np
        N_USERS = 2048
        N_ITEMS = 3072
        EMB = 64
        LN_EPS = 1e-05
        key = jax.random.key(seed)
        ks = jax.random.split(key, 10)
        N = N_USERS + N_ITEMS
        ego = jax.random.normal(ks[0], (N, EMB), jnp.float32)
        adj = (jax.random.uniform(ks[1], (N, N), jnp.float32) < 0.01).astype(jnp.float32) * 0.02
        xav = float(np.sqrt(6.0 / (EMB + EMB)))
        W_u = jax.random.uniform(ks[2], (EMB, EMB), jnp.float32, -xav, xav)
        W_i = jax.random.uniform(ks[3], (EMB, EMB), jnp.float32, -xav, xav)
        diag_u = jax.random.uniform(ks[4], (N_USERS,), jnp.float32, 0.99, 1.01)
        diag_i = jax.random.uniform(ks[5], (N_ITEMS,), jnp.float32, 0.99, 1.01)
        par_u = jax.random.uniform(ks[6], (2,), jnp.float32, 0.0, 0.99)
        par_i = jax.random.uniform(ks[7], (2,), jnp.float32, 0.0, 0.99)
        ln_gamma = jnp.ones((EMB,), jnp.float32)
        ln_beta = jnp.zeros((EMB,), jnp.float32)
        return {'ego_embeddings': ego, 'adj': adj, 'W_u': W_u, 'diag_u': diag_u, 'par_u': par_u, 'W_i': W_i, 'diag_i': diag_i, 'par_i': par_i, 'ln_gamma': ln_gamma, 'ln_beta': ln_beta}
    _L0_gnn_all = _L0_gnn_setup()
    _L0_gnn_in = {k: v for k, v in _L0_gnn_all.items() if k in ('W_u', 'diag_u', 'par_u', 'W_i', 'diag_i', 'par_i', 'ln_gamma', 'ln_beta')}
    del _L0_gnn_all
    return {'x': x, 'adj': adj, 'L0_gnn_W_u': _L0_gnn_in['W_u'], 'L0_gnn_diag_u': _L0_gnn_in['diag_u'], 'L0_gnn_par_u': _L0_gnn_in['par_u'], 'L0_gnn_W_i': _L0_gnn_in['W_i'], 'L0_gnn_diag_i': _L0_gnn_in['diag_i'], 'L0_gnn_par_i': _L0_gnn_in['par_i'], 'L0_gnn_ln_gamma': _L0_gnn_in['ln_gamma'], 'L0_gnn_ln_beta': _L0_gnn_in['ln_beta']}

def reference(x, adj, L0_gnn_W_u, L0_gnn_diag_u, L0_gnn_par_u, L0_gnn_W_i, L0_gnn_diag_i, L0_gnn_par_i, L0_gnn_ln_gamma, L0_gnn_ln_beta):
    import jax
    import jax.numpy as jnp

    def _L0_gnn_ref(ego_embeddings, adj, W_u, diag_u, par_u, W_i, diag_i, par_i, ln_gamma, ln_beta):
        import jax, jax.numpy as jnp
        import numpy as np
        N_USERS = 2048
        N_ITEMS = 3072
        EMB = 64
        LN_EPS = 1e-05
        nu = diag_u.shape[0]
        res = ego_embeddings
        ego_u = ego_embeddings[:nu]
        ego_i = ego_embeddings[nu:]
        u = par_u[0] * par_u[1] * (diag_u[:, None] * ego_u @ W_u) + ego_u
        i = par_i[0] * par_i[1] * (diag_i[:, None] * ego_i @ W_i) + ego_i
        e = jnp.concatenate([u, i], axis=0)
        h = adj @ (adj.T @ e)
        mu = jnp.mean(h, axis=-1, keepdims=True)
        var = jnp.var(h, axis=-1, keepdims=True)
        out = (h - mu) * jax.lax.rsqrt(var + LN_EPS) * ln_gamma + ln_beta + res
        return out
    h = jnp.maximum(_layernorm(x, axis=-1), 0.0)
    x = x + _L0_gnn_ref(h, adj, L0_gnn_W_u, L0_gnn_diag_u, L0_gnn_par_u, L0_gnn_W_i, L0_gnn_diag_i, L0_gnn_par_i, L0_gnn_ln_gamma, L0_gnn_ln_beta)
    return x

_drawn_inputs = setup_inputs


def setup_inputs(seed=0):
    import zlib

    import numpy as np

    out = dict(_drawn_inputs(seed))
    spreads = {'L0_gnn_ln_gamma': (1.0, 0.2), 'L0_gnn_ln_beta': (0.0, 0.1)}
    factors = {}
    for name, (base, spread) in spreads.items():
        noise = np.random.default_rng([zlib.crc32(name.encode()), seed]).standard_normal(out[name].shape)
        drawn = base * np.exp(spread * noise) if base else spread * noise
        out[name] = jnp.asarray(drawn.astype(out[name].dtype))
    for name, factor in factors.items():
        out[name] = (out[name] * factor).astype(out[name].dtype)
    return out
```

```python
from contextlib import ExitStack

import concourse.bass as bass
from concourse import mybir

F32 = mybir.dt.float32
ALU = mybir.AluOpType
ACT = mybir.ActivationFunctionType

P = 128
HALF = 64
Q = 32
GROUPS = P // Q
ROWS = 256
SUB = ROWS // P
RT = ROWS // Q
CACHED = 768
CACHED_BLOCKS = CACHED // P
CHUNK_BLOCKS = [7, 7, 7, 7, 6]
CHUNKS = len(CHUNK_BLOCKS)
WIDE = CHUNK_BLOCKS[0]
SLOTS = CHUNKS
EPS = 1e-5


def gnn_kernel(nc, x, adj, w_u, diag_u, par_u, w_i, diag_i, par_i, gamma, beta, out):
    n, d = x.shape
    users = diag_u.shape[0]
    supers = n // ROWS
    tiles = n // P
    user_tiles = users // P
    blocks = sum(CHUNK_BLOCKS)
    streamed = blocks * P
    assert d == HALF and streamed + CACHED == n and users % ROWS == 0
    panels = [b * P for b in CHUNK_BLOCKS] + [CACHED]
    n_panels = len(panels)
    wide_panels = CHUNK_BLOCKS.count(WIDE)
    rounds = supers // SLOTS
    assert supers % SLOTS == 0 and wide_panels == n_panels - 2 and supers % 2 == 0
    pairs_pass1 = n_panels * supers
    slot_loads = n_panels * rounds
    pre_group = 8
    pre_groups = tiles // pre_group

    x_v = x.rearrange("(s p u) c -> p s u c", p=P, u=SUB)
    out_v = out.rearrange("(s p u) c -> s p u c", p=P, u=SUB)

    ctx = ExitStack()
    with ctx:
        def sb(name, shape):
            return ctx.enter_context(nc.sbuf_tensor(name, shape, F32))

        def ps(name, shape):
            return ctx.enter_context(nc.psum_tensor(name, shape, F32))

        def sem(name):
            return ctx.enter_context(nc.semaphore(name))

        ring = sb("ring", [P, SLOTS, RT * Q * WIDE])
        cache = sb("cache", [P, CACHED_BLOCKS, n])
        stage = sb("stage", [P, 2, CACHED_BLOCKS, ROWS])
        x_sb = sb("x_sb", [P, tiles, d])
        e_sb = sb("e_sb", [P, tiles, d])
        g_sb = sb("g_sb", [P, blocks, d])
        gc_sb = sb("gc_sb", [P, CACHED_BLOCKS, d])
        gT = sb("gT", [P, WIDE * HALF])
        hT = sb("hT", [P, 2, ROWS])
        o_sb = sb("o_sb", [P, 2, SUB, d])
        ident = sb("ident", [P, P])
        ident2 = sb("ident2", [P, d])
        wts = sb("wts", [d, 2, d])
        coef = sb("coef", [P, tiles])
        par = sb("par", [P, 2, 2])
        parp = sb("parp", [P, 2])
        gam = sb("gam", [P, d])
        bet = sb("bet", [P, d])
        eps = sb("eps", [P, 1])
        st = sb("st", [P, SUB, 6])
        mv = sb("mv", [P, SUB, 2])
        sd = sb("sd", [P, SUB])
        rs = sb("rs", [P, SUB])
        spare = stage[:, :, :, :].rearrange("p a b c -> p (a b c)")
        h_sb = spare[:, 0:1024].rearrange("p (b t c) -> p b t c", b=2, c=d)
        hT1 = spare[0:d, 1024:2048].rearrange("p (t c) -> p t c", c=P)
        st1 = spare[:, 2048:2048 + pre_group * 6].rearrange("p (t c) -> p t c", c=6)
        mv1 = spare[:, 2112:2112 + pre_group * 2].rearrange("p (t c) -> p t c", c=2)
        sd1 = spare[:, 2144:2144 + pre_group]
        rs1 = spare[:, 2160:2160 + pre_group]

        bank = [ps(f"bank{b}", [P, 512]) for b in range(2)]
        tr_ps = [ps(f"tr_ps{b}", [P, 3, 512]) for b in range(2)]
        acc1, gb_ps = bank
        hT1_ps = tr_ps[0][0:d, 0:2, :].rearrange("p a (t c) -> p (a t) c", c=P)
        e_ps = tr_ps[0][:, 2, :].rearrange("p (t c) -> p t c", c=d)
        acc2 = [tr_ps[1][:, b, 0:ROWS] for b in range(2)]
        ho_ps = [bank[b][:, 0:SUB * d].rearrange("p (u c) -> p u c", u=SUB) for b in range(2)]

        loaded = [sem(f"loaded{k}") for k in range(SLOTS)]
        used = sem("used")
        turned = sem("turned")
        consts_in = sem("consts_in")
        x_in = [sem(f"x_in{g}") for g in range(pre_groups)]
        ident0 = sem("ident0")
        ident_ok = sem("ident_ok")
        ident2_ok = sem("ident2_ok")
        eps_ok = sem("eps_ok")
        parp_ok = sem("parp_ok")
        coef_ok = sem("coef_ok")
        step1 = sem("step1")
        var1_ok = sem("var1_ok")
        sd1_ok = sem("sd1_ok")
        h_ok = sem("h_ok")
        hT1_done = sem("hT1_done")
        hT1_ok = sem("hT1_ok")
        hw_done = sem("hw_done")
        e_ok = sem("e_ok")
        y_step = sem("y_step")
        gT_ok = sem("gT_ok")
        gb_done = sem("gb_done")
        g_ok = sem("g_ok")
        tr_done = sem("tr_done")
        cache_ok = sem("cache_ok")
        stage_ok = sem("stage_ok")
        acc2_done = sem("acc2_done")
        hT_ok = sem("hT_ok")
        ho_done = sem("ho_done")
        st_ok = sem("st_ok")
        mv_ok = sem("mv_ok")
        sd_ok = sem("sd_ok")
        rs_ok = sem("rs_ok")
        norm_ok = sem("norm_ok")
        scaled_ok = sem("scaled_ok")
        o_ok = sem("o_ok")
        stored = [sem(f"stored{b}") for b in range(2)]

        block = ctx.enter_context(nc.Block())

        def pass1_load(sp, col, width, s, slot):
            src = adj[ROWS * s:ROWS * (s + 1), bass.ds(col, width)].rearrange("(p u) j -> p u j", u=SUB)
            dst = ring[:, slot, 0:SUB * width].rearrange("p (u j) -> p u j", u=SUB)
            sp.dma_start(dst, src).then_inc(loaded[slot], 16)

        def pass2_load(eng, s, k, groups):
            width = Q * CHUNK_BLOCKS[k]
            base = sum(CHUNK_BLOCKS[:k]) * P
            for g in groups:
                src = adj[bass.ds(s * ROWS, ROWS), base + g * width:base + (g + 1) * width]
                dst = ring[Q * g:Q * (g + 1), k, 0:RT * width].rearrange("q (t j) -> q t j", t=RT)
                eng.dma_start(dst, src.rearrange("(t q) j -> q t j", q=Q)).then_inc(loaded[k], 16)

        def uses(s, k):
            return pairs_pass1 + s * CHUNKS + k + 1

        @block.sync
        def _(sp):
            def panel(k, col, width):
                for s in range(supers):
                    if not (isinstance(k, int) and k == 0 and s < SLOTS):
                        sp.wait_ge(used, k * supers + s - SLOTS + 1)
                    pass1_load(sp, col, width, s, s % SLOTS)

            panel(0, 0, panels[0])
            with sp.Fori(1, wide_panels, 1) as k:
                panel(k, k * panels[0], panels[0])
            for k in range(wide_panels, n_panels):
                panel(k, sum(panels[:k]), panels[k])

            def superblock(s, b, store=True):
                for k in range(CHUNKS):
                    sp.wait_ge(used, uses(s - 1, k))
                    pass2_load(sp, s, k, (0, 1))
                if store:
                    sp.wait_ge(o_ok, s - 1)
                    sp.dma_start(out_v[s - 2], o_sb[:, b, :, :]).then_inc(stored[b], 16)

            superblock(0, 0, store=False)
            superblock(1, 1, store=False)
            with sp.Fori(1, supers // 2, 1) as i:
                superblock(i * 2, 0)
                superblock(i * 2 + 1, 1)
            for s in (supers - 2, supers - 1):
                sp.wait_ge(o_ok, s + 1)
                sp.dma_start(out_v[s], o_sb[:, s % 2, :, :]).then_inc(stored[s % 2], 16)
            for b in range(2):
                sp.wait_ge(stored[b], 16 * (supers // 2))

        @block.gpsimd
        def _(pool):
            nc.gpsimd.memset(ident[:], 0.0).then_inc(ident0, 1)
            nc.gpsimd.memset(eps[:], EPS).then_inc(eps_ok, 1)
            pool.wait_ge(ident0, 1)
            nc.gpsimd.affine_select(out=ident[:], in_=ident[:], compare_op=ALU.not_equal, fill=1.0, base=0,
                                    pattern=[[-1, P]], channel_multiplier=1).then_inc(ident_ok, 1)
            pool.wait_ge(ident_ok, 1)
            nc.gpsimd.tensor_tensor(ident2[:], ident[:, 0:d], ident[:, d:P], ALU.add).then_inc(ident2_ok, 1)
            for g in range(pre_groups):
                rows = x_sb[:, g * pre_group:(g + 1) * pre_group, :]
                pool.wait_ge(h_ok, g + 1)
                nc.gpsimd.tensor_tensor(rows, rows, h_sb[:, g % 2, :, :], ALU.add).then_inc(y_step, 1)
                pool.wait_ge(y_step, 2 * g + 1)
                if g == 0:
                    pool.wait_ge(consts_in, 16 * 8)
                wide = bet[:].unsqueeze(1).broadcast_to([P, pre_group, d])
                nc.gpsimd.tensor_tensor(rows, rows, wide, ALU.add).then_inc(y_step, 1)
            pool.wait_ge(y_step, 2 * pre_groups)

            def finish(s, b):
                o = o_sb[:, b, :, :]
                pool.wait_ge(norm_ok, SUB * (s + 1))
                nc.gpsimd.tensor_tensor(o, o, gam[:].unsqueeze(1).broadcast_to([P, SUB, d]),
                                        ALU.mult).then_inc(scaled_ok, 1)
                pool.wait_ge(scaled_ok, s + 1)
                nc.gpsimd.tensor_tensor(o, o, x_sb[:, bass.ds(s * SUB, SUB), :], ALU.add).then_inc(o_ok, 1)

            with pool.Fori(0, supers // 2, 1) as i:
                finish(i * 2, 0)
                finish(i * 2 + 1, 1)

        @block.scalar
        def _(act):
            act.dma_start(x_sb[:, 0:pre_group, :].rearrange("p (s u) c -> p s u c", u=SUB),
                          x_v[:, 0:pre_group // SUB]).then_inc(x_in[0], 16)
            user_diag = diag_u.rearrange("(s p u) -> p s u", p=P, u=SUB)
            item_diag = diag_i.rearrange("(s p u) -> p s u", p=P, u=SUB)
            act.dma_start(coef[:, 0:user_tiles].rearrange("p (s u) -> p s u", u=SUB), user_diag).then_inc(consts_in, 16)
            act.dma_start(coef[:, user_tiles:tiles].rearrange("p (s u) -> p s u", u=SUB),
                          item_diag).then_inc(consts_in, 16)
            act.dma_start(wts[:, 0, :], w_u).then_inc(consts_in, 16)
            act.dma_start(wts[:, 1, :], w_i).then_inc(consts_in, 16)
            act.dma_start(par[:, 0, :], par_u.partition_broadcast(P)).then_inc(consts_in, 16)
            act.dma_start(par[:, 1, :], par_i.partition_broadcast(P)).then_inc(consts_in, 16)
            act.dma_start(gam[:], gamma.partition_broadcast(P)).then_inc(consts_in, 16)
            act.dma_start(bet[:], beta.partition_broadcast(P)).then_inc(consts_in, 16)
            for g in range(1, pre_groups):
                a, b = g * pre_group, (g + 1) * pre_group
                act.dma_start(x_sb[:, a:b, :].rearrange("p (s u) c -> p s u c", u=SUB),
                              x_v[:, a // SUB:b // SUB]).then_inc(x_in[g], 16)
            act.wait_ge(eps_ok, 1)
            for g in range(pre_groups):
                act.wait_ge(var1_ok, g + 1)
                nc.scalar.activation(sd1, mv1[:, :, 1], ACT.Sqrt, bias=eps[:, 0:1]).then_inc(sd1_ok, 1)
                act.wait_ge(hT1_done, g + 1)
                nc.scalar.copy(hT1, hT1_ps).then_inc(hT1_ok, 1)

            def panel_end(k, width, dst, groups=2, from_banks=(gb_ps,)):
                act.wait_ge(used, (k + 1) * supers)
                src = acc1[:, 0:width // 2].rearrange("p (g b q) -> p b g q", g=groups, q=Q)
                to = gT[:, 0:width // 2].rearrange("p (b g q) -> p b g q", g=groups, q=Q)
                nc.scalar.copy(to, src).then_inc(gT_ok, 1)
                act.wait_ge(gb_done, k + 1)
                n_blocks = dst.shape[1] // len(from_banks)
                for m, src in enumerate(from_banks):
                    i = nc.scalar.copy(dst[:, m * n_blocks:(m + 1) * n_blocks, :],
                                       src[:, 0:n_blocks * d].rearrange("p (b c) -> p b c", c=d))
                    i.then_inc(g_ok, 1)

            with act.Fori(0, wide_panels, 1) as k:
                panel_end(k, panels[0], g_sb[:, bass.ds(k * WIDE, WIDE), :])
            for k in range(wide_panels, n_panels - 1):
                first = sum(CHUNK_BLOCKS[:k])
                panel_end(k, panels[k], g_sb[:, first:first + CHUNK_BLOCKS[k], :])

            def keep(s, b):
                act.wait_ge(tr_done, s + 1)
                src = tr_ps[b][:, :, :].rearrange("p a (m u c) -> p (a m) u c", m=2, u=SUB)
                dst = cache[:, :, bass.ds(s * ROWS, ROWS)].rearrange("p m (c u) -> p m u c", u=SUB)
                nc.scalar.copy(dst, src).then_inc(cache_ok, 1)

            def stage_rows(s, b):
                nc.scalar.copy(stage[:, b, :, :], cache[:, :, bass.ds(s * ROWS, ROWS)]).then_inc(stage_ok, 1)

            with act.Fori(0, (supers - SLOTS - 1) // 2, 1) as i:
                keep(i * 2, 0)
                keep(i * 2 + 1, 1)
            for s in range(supers - SLOTS - 1, supers):
                keep(s, s % 2)
                if s >= supers - SLOTS:
                    k = s - (supers - SLOTS)
                    act.wait_ge(used, uses(-1, k))
                    pass2_load(act, 0, k, (2, 3))
            act.wait_ge(cache_ok, supers)
            act.wait_ge(y_step, 2 * pre_groups - 1)
            stage_rows(0, 0)
            panel_end(n_panels - 1, CACHED, gc_sb[:, :, :], groups=1, from_banks=(gb_ps, acc1))

            def superblock(s, b, first=False, load=True):
                def load_next(k):
                    if load:
                        act.wait_ge(used, uses(s, k))
                        pass2_load(act, s + 1, k, (2, 3))

                if not first:
                    act.wait_ge(acc2_done, s)
                    nc.scalar.copy(hT[:, 1 - b, :], acc2[1 - b]).then_inc(hT_ok, 1)
                if load:
                    stage_rows(s + 1, 1 - b)
                load_next(0)
                load_next(1)
                if not first:
                    act.wait_ge(mv_ok, s * SUB)
                    nc.scalar.activation(sd[:], mv[:, :, 1], ACT.Sqrt, bias=eps[:, 0:1]).then_inc(sd_ok, 1)
                for k in range(2, CHUNKS):
                    load_next(k)

            superblock(0, 0, first=True)
            superblock(1, 1)
            with act.Fori(1, supers // 2 - 1, 1) as i:
                superblock(i * 2, 0)
                superblock(i * 2 + 1, 1)
            superblock(supers - 2, 0)
            superblock(supers - 1, 1, load=False)
            act.wait_ge(acc2_done, supers)
            nc.scalar.copy(hT[:, 1, :], acc2[1]).then_inc(hT_ok, 1)
            act.wait_ge(mv_ok, supers * SUB)
            nc.scalar.activation(sd[:], mv[:, :, 1], ACT.Sqrt, bias=eps[:, 0:1]).then_inc(sd_ok, 1)

        @block.vector
        def _(dve):
            steps = 0
            for g in range(pre_groups):
                rows = x_sb[:, g * pre_group:(g + 1) * pre_group, :]
                h = h_sb[:, g % 2, :, :]
                dve.wait_ge(x_in[g], 16)
                for t in range(pre_group):
                    nc.vector.bn_stats(st1[:, t, :], rows[:, t, :]).then_inc(step1, 1)
                steps += pre_group
                dve.wait_ge(step1, steps)
                if g >= 1:
                    dve.wait_ge(sd1_ok, g)
                for t in range(pre_group):
                    i = nc.vector.bn_aggr(mv1[:, t, :], st1[:, t, :])
                    i.then_inc(step1, 1)
                steps += pre_group
                dve.wait_ge(step1, steps)
                if g >= 2:
                    dve.wait_ge(y_step, 2 * (g - 2) + 1)
                nc.vector.tensor_tensor(h, rows, mv1[:, :, 0:1].broadcast_to([P, pre_group, d]),
                                        ALU.subtract).then_inc(var1_ok, 1)
                if g == 0:
                    dve.wait_ge(consts_in, 16 * 8)
                    nc.vector.tensor_tensor(parp[:], par[:, :, 0], par[:, :, 1], ALU.mult).then_inc(parp_ok, 1)
                    dve.wait_ge(parp_ok, 1)
                    nc.vector.tensor_scalar(coef[:, 0:user_tiles], coef[:, 0:user_tiles], parp[:, 0:1], None,
                                            ALU.mult).then_inc(coef_ok, 1)
                    nc.vector.tensor_scalar(coef[:, user_tiles:tiles], coef[:, user_tiles:tiles], parp[:, 1:2],
                                            None, ALU.mult).then_inc(coef_ok, 1)
                    dve.wait_ge(coef_ok, 2)
                dve.wait_ge(sd1_ok, g + 1)
                nc.vector.reciprocal(rs1, sd1).then_inc(step1, 1)
                steps += 1
                dve.wait_ge(step1, steps)
                dve.wait_ge(var1_ok, g + 1)
                nc.vector.scalar_tensor_tensor(out=h, in0=h, scalar=0.0, in1=rs1.unsqueeze(2).broadcast_to(
                    [P, pre_group, d]), op0=ALU.max, op1=ALU.mult).then_inc(h_ok, 1)
                dve.wait_ge(h_ok, g + 1)
                dve.wait_ge(hw_done, g + 1)
                e = e_sb[:, g * pre_group:(g + 1) * pre_group, :]
                c = coef[:, g * pre_group:(g + 1) * pre_group].unsqueeze(2).broadcast_to([P, pre_group, d])
                nc.vector.tensor_tensor(e, e_ps, c, ALU.mult).then_inc(step1, 1)
                steps += 1
                dve.wait_ge(step1, steps)
                nc.vector.tensor_tensor(e, e, h, ALU.add).then_inc(e_ok, 1)

            def turn(s, k):
                dve.wait_ge(loaded[k], 16 * slot_loads + 64 * (s + 1))
                a = ring[:, k, 0:RT * Q * CHUNK_BLOCKS[k]]
                nc.vector.transpose(a, a).then_inc(turned, 1)

            def stats(s, b):
                dve.wait_ge(ho_done, s + 1)
                for u in range(SUB):
                    nc.vector.bn_stats(st[:, u, :], ho_ps[b][:, u, :]).then_inc(st_ok, 1)
                dve.wait_ge(st_ok, SUB * (s + 1))

            def variances():
                for u in range(SUB):
                    nc.vector.bn_aggr(mv[:, u, :], st[:, u, :]).then_inc(mv_ok, 1)

            def normalize(s, b, reused=True):
                dve.wait_ge(sd_ok, s + 1)
                nc.vector.reciprocal(rs[:], sd[:]).then_inc(rs_ok, 1)
                dve.wait_ge(rs_ok, s + 1)
                if reused:
                    dve.wait_ge(stored[b], stored_before(s, b))
                for u in range(SUB):
                    nc.vector.tensor_scalar(o_sb[:, b, u, :], ho_ps[b][:, u, :], mv[:, u, 0:1], rs[:, u:u + 1],
                                            ALU.subtract, ALU.mult).then_inc(norm_ok, 1)

            def stored_before(s, b):
                return 8 * (s - b)

            def superblock(s, b, prev=True, reused=True):
                turn(s, 0)
                turn(s, 1)
                if prev:
                    stats(s - 1, 1 - b)
                turn(s, 2)
                if prev:
                    variances()
                turn(s, 3)
                if prev:
                    normalize(s - 1, 1 - b, reused)
                turn(s, 4)

            superblock(0, 0, prev=False)
            superblock(1, 1, reused=False)
            superblock(2, 0, reused=False)
            superblock(3, 1)
            with dve.Fori(2, supers // 2, 1) as i:
                superblock(i * 2, 0)
                superblock(i * 2 + 1, 1)
            stats(supers - 1, 1)
            variances()
            normalize(supers - 1, 1)

        @block.tensor
        def _(pe):
            def pre_transpose(g):
                pe.wait_ge(h_ok, g + 1)
                if g >= 1:
                    pe.wait_ge(hT1_ok, g)
                for t in range(pre_group):
                    i = nc.tensor.transpose(hT1_ps[:, t, :], h_sb[:, g % 2, t, :], ident[:])
                i.then_inc(hT1_done, 1)

            def pre_weights(g):
                pe.wait_ge(hT1_ok, g + 1)
                if g >= 1:
                    pe.wait_ge(e_ok, g)
                w = wts[:, 0 if g * pre_group < user_tiles else 1, :]
                for t in range(pre_group):
                    i = nc.tensor.matmul(e_ps[:, t, :], hT1[:, t, :], w, start=True, stop=True)
                i.then_inc(hw_done, 1)

            def pair(k, s, width, cached=False):
                slot = s % SLOTS
                pe.wait_ge(loaded[slot], 16 * (k * rounds + s // SLOTS + 1))
                a = ring[:, slot, 0:SUB * width].rearrange("p (u j) -> p u j", u=SUB)
                half = width // 2
                if cached:
                    if s >= 2:
                        pe.wait_ge(cache_ok, s - 1)
                    for u in range(SUB):
                        for m in range(CACHED_BLOCKS):
                            at = (m % 2) * ROWS + u * P
                            i = nc.tensor.transpose(tr_ps[s % 2][:, m // 2, at:at + P],
                                                    a[:, u, m * P:(m + 1) * P], ident[:])
                    i.then_inc(tr_done, 1)
                for u in range(SUB):
                    t = s * SUB + u
                    for c in range(2):
                        i = nc.tensor.matmul(acc1[HALF * c:HALF * (c + 1), 0:half], e_sb[:, t, :],
                                             a[:, u, c * half:(c + 1) * half],
                                             start=(t == 0), stop=(t == tiles - 1))
                i.then_inc(used, 1)

            def turn_back(n_blocks):
                for b in range(n_blocks):
                    for c in range(2):
                        rows = slice(HALF * c, HALF * (c + 1))
                        i = nc.tensor.matmul(gb_ps[rows, b * d:(b + 1) * d], gT[rows, 2 * Q * b:2 * Q * (b + 1)],
                                             ident2[rows, :], start=True, stop=True)
                i.then_inc(gb_done, 1)

            def turn_back_cached(k):
                pe.wait_ge(gT_ok, k + 1)
                pe.wait_ge(g_ok, k)
                for b in range(CACHED_BLOCKS):
                    c, at = divmod(b * P, CACHED // 2)
                    rows = slice(HALF * c, HALF * (c + 1))
                    to = (gb_ps if c == 0 else acc1)[:, at // P * d:(at // P + 1) * d]
                    i = nc.tensor.matmul(to, gT[rows, at:at + P],
                                         ident2[rows, :], start=True, stop=True)
                i.then_inc(gb_done, 1)

            pe.wait_ge(ident_ok, 1)
            pe.wait_ge(consts_in, 16 * 8)
            pre_transpose(0)
            pre_weights(0)
            per = pre_group // SUB
            for s in range(supers):
                if s % per == 0:
                    pe.wait_ge(e_ok, s // per + 1)
                pair(0, s, panels[0])
                if s % per == 0 and s // per + 1 < pre_groups:
                    pre_transpose(s // per + 1)
                if s % per == 1 and s // per + 1 < pre_groups:
                    pre_weights(s // per + 1)
            pe.wait_ge(ident2_ok, 1)

            def panel(k, prev_blocks, width, cached=False):
                pe.wait_ge(gT_ok, k)
                if not (isinstance(k, int) and k == 1):
                    pe.wait_ge(g_ok, k - 1)
                pair(k, 0, width, cached)
                turn_back(prev_blocks)
                for s in range(1, supers):
                    pair(k, s, width, cached)

            panel(1, WIDE, panels[0])
            with pe.Fori(2, wide_panels, 1) as k:
                panel(k, WIDE, panels[0])
            for k in range(wide_panels, n_panels):
                panel(k, CHUNK_BLOCKS[k - 1], panels[k], cached=(k == n_panels - 1))

            def chunk(s, b, k):
                pe.wait_ge(turned, s * CHUNKS + k + 1)
                width = Q * CHUNK_BLOCKS[k]
                a = ring[:, k, 0:RT * width].rearrange("p (t j) -> p t j", t=RT)
                for m in range(CHUNK_BLOCKS[k]):
                    blk = sum(CHUNK_BLOCKS[:k]) + m
                    c = blk % 2
                    i = nc.tensor.matmul(acc2[b][HALF * c:HALF * (c + 1), :], g_sb[:, blk, :],
                                         a[:, :, Q * m:Q * (m + 1)], start=(blk < 2), stop=False)
                i.then_inc(used, 1)

            def cached_part(s, b):
                pe.wait_ge(stage_ok, s + 1)
                for m in range(CACHED_BLOCKS):
                    c = m % 2
                    i = nc.tensor.matmul(acc2[b][HALF * c:HALF * (c + 1), :], gc_sb[:, m, :],
                                         stage[:, b, m, :], start=False, stop=(m >= CACHED_BLOCKS - 2))
                i.then_inc(acc2_done, 1)

            def rows_out(s, b):
                pe.wait_ge(hT_ok, s + 1)
                if not (isinstance(s, int) and s < 2):
                    pe.wait_ge(norm_ok, SUB * (s - 1))
                for u in range(SUB):
                    cols = hT[:, b, :].rearrange("p (c u) -> p u c", u=SUB)[:, u, :]
                    i = nc.tensor.matmul(ho_ps[b][:, u, :], cols, ident2[:], start=True, stop=True)
                i.then_inc(ho_done, 1)

            def superblock(s, b, prev=True):
                chunk(s, b, 0)
                if prev:
                    rows_out(s - 1, 1 - b)
                for k in range(1, CHUNKS):
                    chunk(s, b, k)
                cached_part(s, b)

            pe.wait_ge(cache_ok, supers)
            chunk(0, 0, 0)
            turn_back_cached(n_panels - 1)
            for k in range(1, CHUNKS):
                chunk(0, 0, k)
            pe.wait_ge(g_ok, n_panels + 1)
            cached_part(0, 0)
            superblock(1, 1)
            superblock(2, 0)
            superblock(3, 1)
            with pe.Fori(2, supers // 2, 1) as i:
                superblock(i * 2, 0)
                superblock(i * 2 + 1, 1)
            rows_out(supers - 1, 1)


_INS = ["x", "adj", "L0_gnn_W_u", "L0_gnn_diag_u", "L0_gnn_par_u", "L0_gnn_W_i", "L0_gnn_diag_i",
        "L0_gnn_par_i", "L0_gnn_ln_gamma", "L0_gnn_ln_beta"]


def kernel(**inputs):
    import numpy as _np
    import concourse.bacc as _bacc
    from concourse.bass_utils import run_bass_kernel_spmd as _run

    nc = _bacc.Bacc("TRN2", target_bir_lowering=False, num_devices=1)
    arrays, args = {}, []
    for name in _INS:
        a = _np.ascontiguousarray(inputs[name])
        arrays[f"in_{name}"] = a
        args.append(nc.dram_tensor(f"in_{name}", a.shape, mybir.dt.from_np(a.dtype), kind="ExternalInput").ap())
    result = nc.dram_tensor("result", arrays["in_x"].shape, F32, kind="ExternalOutput").ap()
    gnn_kernel(nc, *args, result)
    r = _run(nc, [arrays], core_ids=[0])
    return r.results[0]["result"]
```

```python
from contextlib import ExitStack

import concourse.bass as bass
from concourse import mybir

F32 = mybir.dt.float32
ALU = mybir.AluOpType
ACT = mybir.ActivationFunctionType

P = 128
HALF = 64
Q = 32
GROUPS = P // Q
ROWS = 256
SUB = ROWS // P
RT = ROWS // Q
PANEL = 1024
PANEL_BLOCKS = PANEL // P
CHUNK_BLOCKS = [7, 7, 7, 6, 6]
CACHE_BLOCKS = [PANEL_BLOCKS - b for b in CHUNK_BLOCKS]
PANELS = CHUNKS = len(CHUNK_BLOCKS)
PAIR_SLOTS = 4
PRE_GROUPS = [2, 6, 8, 8, 8, 8]
PRE_MAX = max(PRE_GROUPS)
EPS = 1e-5


def gnn_kernel(nc, x, adj, w_u, diag_u, par_u, w_i, diag_i, par_i, gamma, beta, out):
    n, d = x.shape
    users = diag_u.shape[0]
    supers = n // ROWS
    tiles = n // P
    user_tiles = users // P
    blocks = sum(CHUNK_BLOCKS)
    cached = sum(CACHE_BLOCKS)
    rounds = supers // PAIR_SLOTS
    pairs = PANELS * supers
    pair_size = SUB * PANEL
    chunk_size = [RT * Q * b for b in CHUNK_BLOCKS]
    chunk_at = [sum(chunk_size[:k]) for k in range(CHUNKS)]
    ring_size = max(PAIR_SLOTS * pair_size, sum(chunk_size))
    assert d == HALF and PANELS * PANEL == n and supers % PAIR_SLOTS == 0 and supers % 2 == 0
    assert sum(PRE_GROUPS) == tiles
    pre_at = [sum(PRE_GROUPS[:g]) for g in range(len(PRE_GROUPS) + 1)]
    assert user_tiles in pre_at
    n_pre = len(PRE_GROUPS)

    x_v = x.rearrange("(s p u) c -> p s u c", p=P, u=SUB)
    out_v = out.rearrange("(s p u) c -> s p u c", p=P, u=SUB)

    ctx = ExitStack()
    with ctx:
        def sb(name, shape):
            return ctx.enter_context(nc.sbuf_tensor(name, shape, F32))

        def sem(name):
            return ctx.enter_context(nc.semaphore(name))

        ring = sb("ring", [P, ring_size])
        cache = sb("cache", [P, cached, n])
        x_sb = sb("x_sb", [P, tiles, d])
        e_all = sb("e_all", [P, tiles * d])
        g_sb = sb("g_sb", [P, blocks, d])
        gc_sb = sb("gc_sb", [P, cached, d])
        ident = sb("ident", [P, P])
        ident2 = sb("ident2", [P, d])
        gam = sb("gam", [P, d])
        eps = sb("eps", [P, 1])
        st = sb("st", [P, SUB, 6])
        mv = sb("mv", [P, SUB, 2])
        sd = sb("sd", [P, SUB])
        rs = sb("rs", [P, SUB])

        e_sb = e_all[:, :].rearrange("p (t c) -> p t c", c=d)
        at_hT = cached * ROWS
        at_o = at_hT + 2 * ROWS
        assert at_o + 2 * SUB * d <= tiles * d
        stage = e_all[:, 0:at_hT].rearrange("p (m c) -> p m c", c=ROWS)
        hT = e_all[:, at_hT:at_o].rearrange("p (b c) -> p b c", b=2)
        o_sb = e_all[:, at_o:at_o + 2 * SUB * d].rearrange("p (b u c) -> p b u c", b=2, u=SUB)
        gT_last = e_all[:, at_hT:at_o]

        place = [0]

        def spare(size, rows=P):
            place[0] += size
            return cache[0:rows, cached - 1, place[0] - size:place[0]]

        h_sb = spare(2 * PRE_MAX * d).rearrange("p (b t c) -> p b t c", b=2, c=d)
        hT1 = spare(PRE_MAX * P, d).rearrange("p (t c) -> p t c", c=P)
        st1 = spare(PRE_MAX * 6).rearrange("p (t c) -> p t c", c=6)
        mv1 = spare(PRE_MAX * 2).rearrange("p (t c) -> p t c", c=2)
        sd1 = spare(PRE_MAX)
        rs1 = spare(PRE_MAX)
        wts = spare(2 * d, d).rearrange("p (w c) -> p w c", w=2)
        coef = spare(tiles)
        par = spare(4).rearrange("p (w c) -> p w c", w=2)
        parp = spare(2)
        bet = spare(d)
        gT_first = cache[:, cached - 1, n - PANEL // 2:n]
        assert place[0] <= n - PANEL // 2

        bank = [ctx.enter_context(nc.psum_tensor(f"bank{b}", [P, 512], F32)) for b in range(7)]
        acc1, gb_ps, tr_ps = bank[0], bank[1], bank[2:4]
        e_ps = bank[6][:, :].rearrange("p (t c) -> p t c", c=d)
        acc2 = [bank[4][:, 0:ROWS], bank[5][:, 0:ROWS]]
        ho_ps = [bank[b][:, 0:SUB * d].rearrange("p (u c) -> p u c", u=SUB) for b in (0, 1)]

        def hT1_bank(t):
            return bank[4 + t // 4][0:d, t % 4 * P:(t % 4 + 1) * P]

        loaded = [sem(f"loaded{k}") for k in range(CHUNKS)]
        used = sem("used")
        turned = sem("turned")
        user_in = sem("user_in")
        par_in = sem("par_in")
        item_in = sem("item_in")
        ln_in = sem("ln_in")
        x_in = [sem(f"x_in{g}") for g in range(n_pre)]
        ident0 = sem("ident0")
        ident_ok = sem("ident_ok")
        ident2_ok = sem("ident2_ok")
        eps_ok = sem("eps_ok")
        parp_ok = sem("parp_ok")
        coef_ok = sem("coef_ok")
        step1 = sem("step1")
        var1_ok = sem("var1_ok")
        sd1_ok = sem("sd1_ok")
        h_ok = sem("h_ok")
        hT1_done = sem("hT1_done")
        hT1_ok = sem("hT1_ok")
        hw_done = sem("hw_done")
        e_ok = sem("e_ok")
        y_step = sem("y_step")
        tr_done = sem("tr_done")
        cache_ok = sem("cache_ok")
        gT_ok = sem("gT_ok")
        gb_done = sem("gb_done")
        g_ok = sem("g_ok")
        stage_ok = sem("stage_ok")
        hT_ok = sem("hT_ok")
        ho_done = sem("ho_done")
        st_ok = sem("st_ok")
        mv_ok = sem("mv_ok")
        sd_ok = sem("sd_ok")
        rs_ok = sem("rs_ok")
        norm_ok = sem("norm_ok")
        scaled_ok = sem("scaled_ok")
        o_ok = sem("o_ok")
        stored = [sem(f"stored{b}") for b in range(2)]

        block = ctx.enter_context(nc.Block())

        def chunk(k, groups=slice(0, P)):
            return ring[groups, chunk_at[k]:chunk_at[k] + chunk_size[k]].rearrange("p (t j) -> p t j", t=RT)

        def pass2_load(eng, s, k, groups):
            width = Q * CHUNK_BLOCKS[k]
            for g in groups:
                col = k * PANEL + g * width + (P * CACHE_BLOCKS[k] if g >= GROUPS // 2 else 0)
                src = adj[bass.ds(s * ROWS, ROWS), col:col + width].rearrange("(t q) j -> q t j", q=Q)
                eng.dma_start(chunk(k, slice(Q * g, Q * (g + 1))), src).then_inc(loaded[k], 16)

        def uses(s, k):
            return pairs + s * CHUNKS + k + 1

        def first_free(k):
            last_slot = min((chunk_at[k] + chunk_size[k] - 1) // pair_size, PAIR_SLOTS - 1)
            return pairs - PAIR_SLOTS + last_slot + 1

        def x_load(eng, g):
            a, b = pre_at[g], pre_at[g + 1]
            eng.dma_start(x_sb[:, a:b, :].rearrange("p (s u) c -> p s u c", u=SUB),
                          x_v[:, a // SUB:b // SUB]).then_inc(x_in[g], 16)

        @block.sync
        def _(sp):
            def panel(k):
                for s in range(supers):
                    if not (isinstance(k, int) and s < PAIR_SLOTS):
                        sp.wait_ge(used, k * supers + s - PAIR_SLOTS + 1)
                    src = adj[ROWS * s:ROWS * (s + 1), bass.ds(k * PANEL, PANEL)]
                    slot = s % PAIR_SLOTS
                    dst = ring[:, slot * pair_size:(slot + 1) * pair_size].rearrange("p (u j) -> p u j", u=SUB)
                    sp.dma_start(dst, src.rearrange("(p u) j -> p u j", u=SUB)).then_inc(loaded[slot], 16)
                    if isinstance(k, int) and 1 <= s + 1 < n_pre:
                        x_load(sp, s + 1)

            x_load(sp, 0)
            panel(0)
            with sp.Fori(1, PANELS, 1) as k:
                panel(k)

            for k in range(CHUNKS):
                sp.wait_ge(used, first_free(k))
                pass2_load(sp, 0, k, (0, 1))

            def superblock(s, b, store=True):
                for k in range(CHUNKS):
                    sp.wait_ge(used, uses(s - 1, k))
                    pass2_load(sp, s, k, (0, 1))
                if store:
                    sp.wait_ge(o_ok, s - 1)
                    sp.dma_start(out_v[s - 2], o_sb[:, b, :, :]).then_inc(stored[b], 16)

            superblock(1, 1, store=False)
            with sp.Fori(1, supers // 2, 1) as i:
                superblock(i * 2, 0)
                superblock(i * 2 + 1, 1)
            for s in (supers - 2, supers - 1):
                sp.wait_ge(o_ok, s + 1)
                sp.dma_start(out_v[s], o_sb[:, s % 2, :, :]).then_inc(stored[s % 2], 16)
            for b in range(2):
                sp.wait_ge(stored[b], 16 * (supers // 2))

        @block.gpsimd
        def _(pool):
            nc.gpsimd.memset(eps[:], EPS).then_inc(eps_ok, 1)
            pool.dma_start(par[:, 0, :], par_u.partition_broadcast(P)).then_inc(par_in, 16)
            pool.dma_start(par[:, 1, :], par_i.partition_broadcast(P)).then_inc(par_in, 16)
            nc.gpsimd.memset(ident[:], 0.0).then_inc(ident0, 1)
            pool.wait_ge(ident0, 1)
            nc.gpsimd.affine_select(out=ident[:], in_=ident[:], compare_op=ALU.not_equal, fill=1.0, base=0,
                                    pattern=[[-1, P]], channel_multiplier=1).then_inc(ident_ok, 1)
            pool.dma_start(gam[:], gamma.partition_broadcast(P)).then_inc(ln_in, 16)
            pool.dma_start(bet, beta.partition_broadcast(P)).then_inc(ln_in, 16)
            pool.wait_ge(ident_ok, 1)
            nc.gpsimd.tensor_tensor(ident2[:], ident[:, 0:d], ident[:, d:P], ALU.add).then_inc(ident2_ok, 1)
            for g in range(n_pre):
                size = PRE_GROUPS[g]
                rows = x_sb[:, pre_at[g]:pre_at[g + 1], :]
                pool.wait_ge(h_ok, g + 1)
                nc.gpsimd.tensor_tensor(rows, rows, h_sb[:, g % 2, 0:size, :], ALU.add).then_inc(y_step, 1)
                if g == 0:
                    pool.wait_ge(ln_in, 32)
                pool.wait_ge(y_step, 2 * g + 1)
                nc.gpsimd.tensor_tensor(rows, rows, bet.unsqueeze(1).broadcast_to([P, size, d]),
                                        ALU.add).then_inc(y_step, 1)
            pool.wait_ge(y_step, 2 * n_pre)

            def finish(s, b):
                o = o_sb[:, b, :, :]
                pool.wait_ge(norm_ok, SUB * (s + 1))
                nc.gpsimd.tensor_tensor(o, o, gam[:].unsqueeze(1).broadcast_to([P, SUB, d]),
                                        ALU.mult).then_inc(scaled_ok, 1)
                pool.wait_ge(scaled_ok, s + 1)
                nc.gpsimd.tensor_tensor(o, o, x_sb[:, bass.ds(s * SUB, SUB), :], ALU.add).then_inc(o_ok, 1)

            with pool.Fori(0, supers // 2, 1) as i:
                finish(i * 2, 0)
                finish(i * 2 + 1, 1)

        @block.scalar
        def _(act):
            coef_u = coef[:, 0:user_tiles].rearrange("p (s u) -> p s u", u=SUB)
            coef_i = coef[:, user_tiles:tiles].rearrange("p (s u) -> p s u", u=SUB)
            act.dma_start(coef_u, diag_u.rearrange("(s p u) -> p s u", p=P, u=SUB)).then_inc(user_in, 16)
            act.dma_start(wts[:, 0, :], w_u).then_inc(user_in, 16)
            act.wait_ge(eps_ok, 1)

            def pre_sd(g):
                act.wait_ge(var1_ok, g + 1)
                nc.scalar.activation(sd1[:, 0:PRE_GROUPS[g]], mv1[:, 0:PRE_GROUPS[g], 1], ACT.Sqrt,
                                     bias=eps[:, 0:1]).then_inc(sd1_ok, 1)

            def pre_copy(g):
                act.wait_ge(hT1_done, g + 1)
                for a in range(0, PRE_GROUPS[g], 4):
                    size = min(4, PRE_GROUPS[g] - a)
                    i = nc.scalar.copy(hT1[:, a:a + size, :],
                                       bank[4 + a // 4][0:d, 0:size * P].rearrange("p (t c) -> p t c", c=P))
                i.then_inc(hT1_ok, 1)

            def keep(k, s, b):
                act.wait_ge(tr_done, k * supers + s + 1)
                first, size = sum(CACHE_BLOCKS[:k]), CACHE_BLOCKS[k]
                src = tr_ps[b][:, 0:size * ROWS].rearrange("p (m u c) -> p m u c", m=size, u=SUB)
                dst = cache[:, first:first + size, bass.ds(s * ROWS, ROWS)].rearrange("p m (c u) -> p m u c", u=SUB)
                nc.scalar.copy(dst, src).then_inc(cache_ok, 1)

            def panel_end(k):
                act.wait_ge(used, (k + 1) * supers)
                gT = gT_first if k < PANELS - 1 else gT_last
                nb, nk = CHUNK_BLOCKS[k], CACHE_BLOCKS[k]
                for c in range(2):
                    half = acc1[HALF * c:HALF * (c + 1), :]
                    at = HALF * nk * c
                    groups = half[:, at:at + 2 * Q * nb].rearrange("p (g b q) -> p b g q", g=2, q=Q)
                    at = 2 * Q * nb * (1 - c)
                    kept = half[:, at:at + HALF * nk].rearrange("p (q m) -> p m q", m=nk)
                    to = gT[HALF * c:HALF * (c + 1), :]
                    nc.scalar.copy(to[:, 0:2 * Q * nb].rearrange("p (b g q) -> p b g q", g=2, q=Q),
                                   groups).then_inc(gT_ok, 1)
                    nc.scalar.copy(to[:, 2 * Q * nb:].rearrange("p (m q) -> p m q", m=nk),
                                   kept).then_inc(gT_ok, 1)
                act.wait_ge(gb_done, k + 1)
                src = gb_ps[:, :].rearrange("p (b c) -> p b c", c=d)
                first, first_kept = sum(CHUNK_BLOCKS[:k]), sum(CACHE_BLOCKS[:k])
                nc.scalar.copy(g_sb[:, first:first + nb, :], src[:, 0:nb, :]).then_inc(g_ok, 1)
                nc.scalar.copy(gc_sb[:, first_kept:first_kept + nk, :], src[:, nb:, :]).then_inc(g_ok, 1)

            pre_sd(0)
            pre_copy(0)
            pre_sd(1)
            act.dma_start(coef_i, diag_i.rearrange("(s p u) -> p s u", p=P, u=SUB)).then_inc(item_in, 16)
            act.dma_start(wts[:, 1, :], w_i).then_inc(item_in, 16)
            pre_copy(1)
            pre_sd(2)
            for g in range(n_pre):
                for s in range(pre_at[g] // SUB, pre_at[g + 1] // SUB):
                    keep(0, s, s % 2)
                if g + 2 < n_pre:
                    pre_copy(g + 2)
                if g + 3 < n_pre:
                    pre_sd(g + 3)
            panel_end(0)
            for k in range(1, PANELS):
                if k == PANELS - 1:
                    act.wait_ge(y_step, 2 * n_pre)
                with act.Fori(0, (supers - PAIR_SLOTS) // 2, 1) as i:
                    keep(k, i * 2, 0)
                    keep(k, i * 2 + 1, 1)
                for s in range(supers - PAIR_SLOTS, supers):
                    keep(k, s, s % 2)
                    if k == PANELS - 1:
                        for m in range(CHUNKS):
                            if first_free(m) == pairs - supers + s + 1:
                                act.wait_ge(used, first_free(m))
                                pass2_load(act, 0, m, (2, 3))
                panel_end(k)

            def stage_rows(s):
                nc.scalar.copy(stage, cache[:, :, bass.ds(s * ROWS, ROWS)]).then_inc(stage_ok, 1)

            def superblock(s, b, first=False, load=True):
                def load_next(k):
                    if load:
                        act.wait_ge(used, uses(s, k))
                        pass2_load(act, s + 1, k, (2, 3))

                if not first:
                    act.wait_ge(used, uses(s - 1, CHUNKS - 1))
                    nc.scalar.copy(hT[:, 1 - b, :], acc2[1 - b]).then_inc(hT_ok, 1)
                stage_rows(s)
                load_next(0)
                load_next(1)
                if not first:
                    act.wait_ge(mv_ok, s * SUB)
                    nc.scalar.activation(sd[:], mv[:, :, 1], ACT.Sqrt, bias=eps[:, 0:1]).then_inc(sd_ok, 1)
                for k in range(2, CHUNKS):
                    load_next(k)

            act.wait_ge(cache_ok, pairs)
            superblock(0, 0, first=True)
            superblock(1, 1)
            with act.Fori(1, supers // 2 - 1, 1) as i:
                superblock(i * 2, 0)
                superblock(i * 2 + 1, 1)
            superblock(supers - 2, 0)
            superblock(supers - 1, 1, load=False)
            act.wait_ge(used, uses(supers - 1, CHUNKS - 1))
            nc.scalar.copy(hT[:, 1, :], acc2[1]).then_inc(hT_ok, 1)
            act.wait_ge(mv_ok, supers * SUB)
            nc.scalar.activation(sd[:], mv[:, :, 1], ACT.Sqrt, bias=eps[:, 0:1]).then_inc(sd_ok, 1)

        @block.vector
        def _(dve):
            steps = [0]

            def step(i):
                i.then_inc(step1, 1)
                steps[0] += 1

            def pre_norm(g):
                size = PRE_GROUPS[g]
                rows = x_sb[:, pre_at[g]:pre_at[g + 1], :]
                h = h_sb[:, g % 2, 0:size, :]
                dve.wait_ge(x_in[g], 16)
                for t in range(size):
                    step(nc.vector.bn_stats(st1[:, t, :], rows[:, t, :]))
                dve.wait_ge(step1, steps[0])
                for t in range(size):
                    step(nc.vector.bn_aggr(mv1[:, t, :], st1[:, t, :]))
                if g >= 2:
                    dve.wait_ge(y_step, 2 * (g - 2) + 1)
                dve.wait_ge(step1, steps[0])
                nc.vector.tensor_tensor(h, rows, mv1[:, 0:size, 0:1].broadcast_to([P, size, d]),
                                        ALU.subtract).then_inc(var1_ok, 1)
                dve.wait_ge(sd1_ok, g + 1)
                step(nc.vector.reciprocal(rs1[:, 0:size], sd1[:, 0:size]))
                dve.wait_ge(var1_ok, g + 1)
                dve.wait_ge(step1, steps[0])
                nc.vector.scalar_tensor_tensor(
                    out=h, in0=h, scalar=0.0, in1=rs1[:, 0:size].unsqueeze(2).broadcast_to([P, size, d]),
                    op0=ALU.max, op1=ALU.mult).then_inc(h_ok, 1)

            def pre_e(g):
                size = PRE_GROUPS[g]
                e = e_sb[:, pre_at[g]:pre_at[g + 1], :]
                dve.wait_ge(h_ok, g + 1)
                dve.wait_ge(hw_done, g + 1)
                c = coef[:, pre_at[g]:pre_at[g + 1]].unsqueeze(2).broadcast_to([P, size, d])
                step(nc.vector.tensor_tensor(e, e_ps[:, 0:size, :], c, ALU.mult))
                dve.wait_ge(step1, steps[0])
                nc.vector.tensor_tensor(e, e, h_sb[:, g % 2, 0:size, :], ALU.add).then_inc(e_ok, 1)

            pre_norm(0)
            dve.wait_ge(par_in, 16 * 2)
            nc.vector.tensor_tensor(parp, par[:, :, 0], par[:, :, 1], ALU.mult).then_inc(parp_ok, 1)
            dve.wait_ge(user_in, 16 * 2)
            dve.wait_ge(parp_ok, 1)
            nc.vector.tensor_scalar(coef[:, 0:user_tiles], coef[:, 0:user_tiles], parp[:, 0:1], None,
                                    ALU.mult).then_inc(coef_ok, 1)
            dve.wait_ge(coef_ok, 1)
            for g in range(1, n_pre):
                pre_norm(g)
                if pre_at[g] == user_tiles:
                    dve.wait_ge(item_in, 16 * 2)
                    nc.vector.tensor_scalar(coef[:, user_tiles:tiles], coef[:, user_tiles:tiles], parp[:, 1:2],
                                            None, ALU.mult).then_inc(coef_ok, 1)
                    dve.wait_ge(coef_ok, 2)
                pre_e(g - 1)
            pre_e(n_pre - 1)

            def turn(s, k):
                dve.wait_ge(loaded[k], (16 * PANELS * rounds if k < PAIR_SLOTS else 0) + 16 * GROUPS * (s + 1))
                a = ring[:, chunk_at[k]:chunk_at[k] + chunk_size[k]]
                nc.vector.transpose(a, a).then_inc(turned, 1)

            def stats(s, b):
                dve.wait_ge(ho_done, s + 1)
                for u in range(SUB):
                    nc.vector.bn_stats(st[:, u, :], ho_ps[b][:, u, :]).then_inc(st_ok, 1)
                dve.wait_ge(st_ok, SUB * (s + 1))

            def variances():
                for u in range(SUB):
                    nc.vector.bn_aggr(mv[:, u, :], st[:, u, :]).then_inc(mv_ok, 1)

            def normalize(s, b, reused=True):
                dve.wait_ge(sd_ok, s + 1)
                nc.vector.reciprocal(rs[:], sd[:]).then_inc(rs_ok, 1)
                if reused:
                    dve.wait_ge(stored[b], 8 * (s - b))
                dve.wait_ge(rs_ok, s + 1)
                for u in range(SUB):
                    nc.vector.tensor_scalar(o_sb[:, b, u, :], ho_ps[b][:, u, :], mv[:, u, 0:1], rs[:, u:u + 1],
                                            ALU.subtract, ALU.mult).then_inc(norm_ok, 1)

            def superblock(s, b, prev=True, reused=True):
                turn(s, 0)
                turn(s, 1)
                if prev:
                    stats(s - 1, 1 - b)
                turn(s, 2)
                if prev:
                    variances()
                turn(s, 3)
                if prev:
                    normalize(s - 1, 1 - b, reused)
                turn(s, 4)

            superblock(0, 0, prev=False)
            superblock(1, 1, reused=False)
            superblock(2, 0, reused=False)
            superblock(3, 1)
            with dve.Fori(2, supers // 2, 1) as i:
                superblock(i * 2, 0)
                superblock(i * 2 + 1, 1)
            stats(supers - 1, 1)
            variances()
            normalize(supers - 1, 1)

        @block.tensor
        def _(pe):
            def pre_transpose(g):
                pe.wait_ge(h_ok, g + 1)
                if g >= 1:
                    pe.wait_ge(hT1_ok, g)
                for t in range(PRE_GROUPS[g]):
                    i = nc.tensor.transpose(hT1_bank(t), h_sb[:, g % 2, t, :], ident[:])
                i.then_inc(hT1_done, 1)

            def pre_weights(g):
                if g == 0:
                    pe.wait_ge(user_in, 16 * 2)
                if pre_at[g] == user_tiles:
                    pe.wait_ge(item_in, 16 * 2)
                if g >= 1:
                    pe.wait_ge(e_ok, g)
                pe.wait_ge(hT1_ok, g + 1)
                w = wts[:, 0 if pre_at[g] < user_tiles else 1, :]
                for t in range(PRE_GROUPS[g]):
                    i = nc.tensor.matmul(e_ps[:, t, :], hT1[:, t, :], w, start=True, stop=True)
                i.then_inc(hw_done, 1)

            def pair(k, s, n_cached):
                slot = s % PAIR_SLOTS
                a = ring[:, slot * pair_size:(slot + 1) * pair_size].rearrange("p (u j) -> p u j", u=SUB)
                mid = (PANEL - n_cached * P) // 2
                if not (isinstance(k, int) and k == 0 and s < 2):
                    pe.wait_ge(cache_ok, k * supers + s - 1)
                pe.wait_ge(loaded[slot], 16 * (k * rounds + s // PAIR_SLOTS + 1))
                for m in range(n_cached):
                    for u in range(SUB):
                        at = m * ROWS + u * P
                        cols = a[:, u, mid:mid + n_cached * P].rearrange("p (c m) -> p m c", m=n_cached)[:, m, :]
                        i = nc.tensor.transpose(tr_ps[s % 2][:, at:at + P], cols, ident[:])
                i.then_inc(tr_done, 1)
                for u in range(SUB):
                    t = s * SUB + u
                    for c in range(2):
                        i = nc.tensor.matmul(acc1[HALF * c:HALF * (c + 1), :], e_sb[:, t, :],
                                             a[:, u, c * (PANEL // 2):(c + 1) * (PANEL // 2)],
                                             start=(t == 0), stop=(t == tiles - 1))
                i.then_inc(used, 1)

            def turn_back(gT):
                for b in range(PANEL_BLOCKS):
                    for c in range(2):
                        rows = slice(HALF * c, HALF * (c + 1))
                        i = nc.tensor.matmul(gb_ps[rows, b * d:(b + 1) * d], gT[rows, HALF * b:HALF * (b + 1)],
                                             ident2[rows, :], start=True, stop=True)
                i.then_inc(gb_done, 1)

            pe.wait_ge(ident_ok, 1)
            pre_transpose(0)
            pre_weights(0)
            pre_transpose(1)
            pre_weights(1)
            for g in range(n_pre):
                pe.wait_ge(e_ok, g + 1)
                first, end = pre_at[g] // SUB, pre_at[g + 1] // SUB
                pair(0, first, CACHE_BLOCKS[0])
                if 1 <= g < n_pre - 1:
                    pre_weights(g + 1)
                for s in range(first + 1, end):
                    pair(0, s, CACHE_BLOCKS[0])
                if g + 2 < n_pre:
                    pre_transpose(g + 2)
            pe.wait_ge(ident2_ok, 1)

            def panel(k, n_cached):
                pe.wait_ge(gT_ok, 4 * k)
                pair(k, 0, n_cached)
                turn_back(gT_first)
                for s in range(1, supers):
                    pair(k, s, n_cached)

            for n_cached in sorted(set(CACHE_BLOCKS)):
                first = max(1, CACHE_BLOCKS.index(n_cached))
                with pe.Fori(first, CACHE_BLOCKS.index(n_cached) + CACHE_BLOCKS.count(n_cached), 1) as k:
                    panel(k, n_cached)

            def multiply(s, b, k):
                pe.wait_ge(turned, s * CHUNKS + k + 1)
                a = chunk(k)
                for m in range(CHUNK_BLOCKS[k]):
                    blk = sum(CHUNK_BLOCKS[:k]) + m
                    c = blk % 2
                    i = nc.tensor.matmul(acc2[b][HALF * c:HALF * (c + 1), :], g_sb[:, blk, :],
                                         a[:, :, Q * m:Q * (m + 1)], start=(blk < 2), stop=(blk >= blocks - 2))
                i.then_inc(used, 1)
                return i

            def multiply_cached(s, b):
                pe.wait_ge(stage_ok, s + 1)
                for m in range(cached):
                    c = m % 2
                    nc.tensor.matmul(acc2[b][HALF * c:HALF * (c + 1), :], gc_sb[:, m, :],
                                     stage[:, m, :], start=False, stop=False)

            def rows_out(s, b):
                pe.wait_ge(hT_ok, s + 1)
                if not (isinstance(s, int) and s < 2):
                    pe.wait_ge(norm_ok, SUB * (s - 1))
                for u in range(SUB):
                    cols = hT[:, b, :].rearrange("p (c u) -> p u c", u=SUB)[:, u, :]
                    i = nc.tensor.matmul(ho_ps[b][:, u, :], cols, ident2[:], start=True, stop=True)
                i.then_inc(ho_done, 1)

            def superblock(s, b):
                multiply(s, b, 0)
                rows_out(s - 1, 1 - b)
                multiply(s, b, 1)
                multiply(s, b, 2)
                multiply_cached(s, b)
                multiply(s, b, 3)
                multiply(s, b, 4)

            multiply(0, 0, 0)
            pe.wait_ge(gT_ok, 4 * PANELS)
            turn_back(gT_last)
            multiply(0, 0, 1)
            multiply(0, 0, 2)
            pe.wait_ge(g_ok, 2 * PANELS)
            multiply_cached(0, 0)
            multiply(0, 0, 3)
            multiply(0, 0, 4)
            superblock(1, 1)
            superblock(2, 0)
            superblock(3, 1)
            with pe.Fori(2, supers // 2, 1) as i:
                superblock(i * 2, 0)
                superblock(i * 2 + 1, 1)
            rows_out(supers - 1, 1)


_INS = ["x", "adj", "L0_gnn_W_u", "L0_gnn_diag_u", "L0_gnn_par_u", "L0_gnn_W_i", "L0_gnn_diag_i",
        "L0_gnn_par_i", "L0_gnn_ln_gamma", "L0_gnn_ln_beta"]


def kernel(**inputs):
    import numpy as _np
    import concourse.bacc as _bacc
    from concourse.bass_utils import run_bass_kernel_spmd as _run

    nc = _bacc.Bacc("TRN2", target_bir_lowering=False, num_devices=1)
    arrays, args = {}, []
    for name in _INS:
        a = _np.ascontiguousarray(inputs[name])
        arrays[f"in_{name}"] = a
        args.append(nc.dram_tensor(f"in_{name}", a.shape, mybir.dt.from_np(a.dtype), kind="ExternalInput").ap())
    result = nc.dram_tensor("result", arrays["in_x"].shape, F32, kind="ExternalOutput").ap()
    gnn_kernel(nc, *args, result)
    r = _run(nc, [arrays], core_ids=[0])
    return r.results[0]["result"]
```

```python
from contextlib import ExitStack

import concourse.bass as bass
from concourse import mybir

F32 = mybir.dt.float32
ALU = mybir.AluOpType
ACT = mybir.ActivationFunctionType

P = 128
HALF = 64
Q = 32
GROUPS = P // Q
ROWS = 256
SUB = ROWS // P
RT = ROWS // Q
PANEL = 1024
PANEL_BLOCKS = PANEL // P
CHUNK_BLOCKS = [8, 7, 6, 6, 6]
CACHE_BLOCKS = [PANEL_BLOCKS - b for b in CHUNK_BLOCKS]
BARE = CACHE_BLOCKS.count(0)
PANELS = CHUNKS = len(CHUNK_BLOCKS)
PAIR_SLOTS = 4
PRE_GROUPS = [2, 4, 4, 6, 8, 8, 8]
LAST_PART = 3
PRE_MAX = max(PRE_GROUPS)
EPS = 1e-5


def gnn_kernel(nc, x, adj, w_u, diag_u, par_u, w_i, diag_i, par_i, gamma, beta, out):
    n, d = x.shape
    users = diag_u.shape[0]
    supers = n // ROWS
    tiles = n // P
    user_tiles = users // P
    blocks = sum(CHUNK_BLOCKS)
    cached = sum(CACHE_BLOCKS)
    rounds = supers // PAIR_SLOTS
    pairs = PANELS * supers
    pair_size = SUB * PANEL
    chunk_size = [RT * Q * b for b in CHUNK_BLOCKS]
    chunk_at = [sum(chunk_size[:k]) for k in range(CHUNKS)]
    ring_size = max(PAIR_SLOTS * pair_size, sum(chunk_size))
    assert d == HALF and PANELS * PANEL == n and supers % PAIR_SLOTS == 0 and supers % 2 == 0
    assert sum(PRE_GROUPS) == tiles and BARE == 1 and CACHE_BLOCKS == sorted(CACHE_BLOCKS)
    pre_at = [sum(PRE_GROUPS[:g]) for g in range(len(PRE_GROUPS) + 1)]
    assert user_tiles in pre_at
    n_pre = len(PRE_GROUPS)

    x_v = x.rearrange("(s p u) c -> p s u c", p=P, u=SUB)
    out_v = out.rearrange("(s p u) c -> s p u c", p=P, u=SUB)

    ctx = ExitStack()
    with ctx:
        def sb(name, shape):
            return ctx.enter_context(nc.sbuf_tensor(name, shape, F32))

        def sem(name):
            return ctx.enter_context(nc.semaphore(name))

        ring = sb("ring", [P, ring_size])
        cache = sb("cache", [P, cached, n])
        x_sb = sb("x_sb", [P, tiles, d])
        e_all = sb("e_all", [P, tiles * d])
        g_sb = sb("g_sb", [P, blocks, d])
        gc_sb = sb("gc_sb", [P, cached, d])
        ident = sb("ident", [P, P])
        ident2 = sb("ident2", [P, d])
        gam = sb("gam", [P, d])
        eps = sb("eps", [P, 1])
        st = sb("st", [P, SUB, 6])
        mv = sb("mv", [P, SUB, 2])
        sd = sb("sd", [P, SUB])
        rs = sb("rs", [P, SUB])

        e_sb = e_all[:, :].rearrange("p (t c) -> p t c", c=d)
        at_hT = cached * ROWS
        at_o = at_hT + 2 * ROWS
        assert at_o + 2 * SUB * d <= tiles * d
        stage = e_all[:, 0:at_hT].rearrange("p (m c) -> p m c", c=ROWS)
        hT = e_all[:, at_hT:at_o].rearrange("p (b c) -> p b c", b=2)
        o_sb = e_all[:, at_o:at_o + 2 * SUB * d].rearrange("p (b u c) -> p b u c", b=2, u=SUB)
        gT_last = e_all[:, at_hT:at_o]

        place = [0]

        def spare(size, rows=P):
            place[0] += size
            return cache[0:rows, cached - 1, place[0] - size:place[0]]

        h_sb = spare(2 * PRE_MAX * d).rearrange("p (b t c) -> p b t c", b=2, c=d)
        hT1 = spare(PRE_MAX * P, d).rearrange("p (t c) -> p t c", c=P)
        st1 = spare(PRE_MAX * 6).rearrange("p (t c) -> p t c", c=6)
        mv1 = spare(PRE_MAX * 2).rearrange("p (t c) -> p t c", c=2)
        sd1 = spare(PRE_MAX)
        rs1 = spare(PRE_MAX)
        wts = spare(2 * d, d).rearrange("p (w c) -> p w c", w=2)
        coef = spare(tiles)
        par = spare(4).rearrange("p (w c) -> p w c", w=2)
        parp = spare(2)
        bet = spare(d)
        gT_first = cache[:, cached - 1, n - PANEL // 2:n]
        assert place[0] <= n - PANEL // 2

        bank = [ctx.enter_context(nc.psum_tensor(f"bank{b}", [P, 512], F32)) for b in range(7)]
        acc1, gb_ps, tr_ps = bank[0], bank[1], bank[2:4]
        e_ps = bank[6][:, :].rearrange("p (t c) -> p t c", c=d)
        acc2 = [bank[4][:, 0:ROWS], bank[5][:, 0:ROWS]]
        ho_ps = [bank[b][:, 0:SUB * d].rearrange("p (u c) -> p u c", u=SUB) for b in (0, 1)]

        def hT1_bank(t):
            return bank[4 + t // 4][0:d, t % 4 * P:(t % 4 + 1) * P]

        loaded = [sem(f"loaded{k}") for k in range(CHUNKS)]
        used = sem("used")
        turned = sem("turned")
        user_in = sem("user_in")
        par_in = sem("par_in")
        item_in = sem("item_in")
        ln_in = sem("ln_in")
        x_in = [sem(f"x_in{g}") for g in range(n_pre)]
        ident0 = sem("ident0")
        ident_ok = sem("ident_ok")
        ident2_ok = sem("ident2_ok")
        eps_ok = sem("eps_ok")
        parp_ok = sem("parp_ok")
        coef_ok = sem("coef_ok")
        step1 = sem("step1")
        var1_ok = sem("var1_ok")
        sd1_ok = sem("sd1_ok")
        h_ok = sem("h_ok")
        hT1_done = sem("hT1_done")
        hT1_ok = sem("hT1_ok")
        hw_done = sem("hw_done")
        e_ok = sem("e_ok")
        y_step = sem("y_step")
        tr_done = sem("tr_done")
        cache_ok = sem("cache_ok")
        gT_ok = sem("gT_ok")
        gb_done = sem("gb_done")
        g_ok = sem("g_ok")
        stage_used = sem("stage_used")
        stage_ok = sem("stage_ok")
        hT_ok = sem("hT_ok")
        ho_done = sem("ho_done")
        st_ok = sem("st_ok")
        mv_ok = sem("mv_ok")
        sd_ok = sem("sd_ok")
        rs_ok = sem("rs_ok")
        scaled_ok = sem("scaled_ok")
        o_ok = sem("o_ok")
        stored = [sem(f"stored{b}") for b in range(2)]

        block = ctx.enter_context(nc.Block())

        def chunk(k, groups=slice(0, P)):
            return ring[groups, chunk_at[k]:chunk_at[k] + chunk_size[k]].rearrange("p (t j) -> p t j", t=RT)

        def pass2_load(eng, s, k, groups):
            width = Q * CHUNK_BLOCKS[k]
            for g in groups:
                col = k * PANEL + g * width + (P * CACHE_BLOCKS[k] if g >= GROUPS // 2 else 0)
                src = adj[bass.ds(s * ROWS, ROWS), col:col + width].rearrange("(t q) j -> q t j", q=Q)
                eng.dma_start(chunk(k, slice(Q * g, Q * (g + 1))), src).then_inc(loaded[k], 16)

        def uses(s, k):
            return pairs + s * CHUNKS + k + 1

        def first_free(k):
            last_slot = min((chunk_at[k] + chunk_size[k] - 1) // pair_size, PAIR_SLOTS - 1)
            return pairs - PAIR_SLOTS + last_slot + 1

        def x_load(eng, g):
            a, b = pre_at[g], pre_at[g + 1]
            eng.dma_start(x_sb[:, a:b, :].rearrange("p (s u) c -> p s u c", u=SUB),
                          x_v[:, a // SUB:b // SUB]).then_inc(x_in[g], 16)

        @block.sync
        def _(sp):
            def panel(k):
                for s in range(supers):
                    if not (isinstance(k, int) and s < PAIR_SLOTS):
                        sp.wait_ge(used, k * supers + s - PAIR_SLOTS + 1)
                    src = adj[ROWS * s:ROWS * (s + 1), bass.ds(k * PANEL, PANEL)]
                    slot = s % PAIR_SLOTS
                    dst = ring[:, slot * pair_size:(slot + 1) * pair_size].rearrange("p (u j) -> p u j", u=SUB)
                    sp.dma_start(dst, src.rearrange("(p u) j -> p u j", u=SUB)).then_inc(loaded[slot], 16)
                    if isinstance(k, int) and 1 <= s + 1 < n_pre:
                        x_load(sp, s + 1)

            x_load(sp, 0)
            panel(0)
            with sp.Fori(1, PANELS, 1) as k:
                panel(k)

            for k in range(CHUNKS):
                sp.wait_ge(used, first_free(k))
                pass2_load(sp, 0, k, (0, 1))

            def superblock(s, b, store=True):
                for k in range(CHUNKS):
                    sp.wait_ge(used, uses(s - 1, k))
                    pass2_load(sp, s, k, (0, 1))
                if store:
                    sp.wait_ge(o_ok, SUB * (s - 1))
                    sp.dma_start(out_v[s - 2], o_sb[:, b, :, :]).then_inc(stored[b], 16)

            superblock(1, 1, store=False)
            with sp.Fori(1, supers // 2, 1) as i:
                superblock(i * 2, 0)
                superblock(i * 2 + 1, 1)
            for s in (supers - 2, supers - 1):
                sp.wait_ge(o_ok, SUB * (s + 1))
                sp.dma_start(out_v[s], o_sb[:, s % 2, :, :]).then_inc(stored[s % 2], 16)
            for b in range(2):
                sp.wait_ge(stored[b], 16 * (supers // 2))

        @block.gpsimd
        def _(pool):
            nc.gpsimd.memset(eps[:], EPS).then_inc(eps_ok, 1)
            pool.dma_start(par[:, 0, :], par_u.partition_broadcast(P)).then_inc(par_in, 16)
            pool.dma_start(par[:, 1, :], par_i.partition_broadcast(P)).then_inc(par_in, 16)
            nc.gpsimd.memset(ident[:], 0.0).then_inc(ident0, 1)
            pool.wait_ge(ident0, 1)
            nc.gpsimd.affine_select(out=ident[:], in_=ident[:], compare_op=ALU.not_equal, fill=1.0, base=0,
                                    pattern=[[-1, P]], channel_multiplier=1).then_inc(ident_ok, 1)
            pool.dma_start(gam[:], gamma.partition_broadcast(P)).then_inc(ln_in, 16)
            pool.dma_start(bet, beta.partition_broadcast(P)).then_inc(ln_in, 16)
            pool.wait_ge(ident_ok, 1)
            nc.gpsimd.tensor_tensor(ident2[:], ident[:, 0:d], ident[:, d:P], ALU.add).then_inc(ident2_ok, 1)
            for g in range(n_pre):
                size = PRE_GROUPS[g]
                rows = x_sb[:, pre_at[g]:pre_at[g + 1], :]
                pool.wait_ge(h_ok, g + 1)
                nc.gpsimd.tensor_tensor(rows, rows, h_sb[:, g % 2, 0:size, :], ALU.add).then_inc(y_step, 1)
                if g == 0:
                    pool.wait_ge(ln_in, 32)
                pool.wait_ge(y_step, 2 * g + 1)
                nc.gpsimd.tensor_tensor(rows, rows, bet.unsqueeze(1).broadcast_to([P, size, d]),
                                        ALU.add).then_inc(y_step, 1)

        @block.scalar
        def _(act):
            coef_u = coef[:, 0:user_tiles].rearrange("p (s u) -> p s u", u=SUB)
            coef_i = coef[:, user_tiles:tiles].rearrange("p (s u) -> p s u", u=SUB)
            act.dma_start(coef_u, diag_u.rearrange("(s p u) -> p s u", p=P, u=SUB)).then_inc(user_in, 16)
            act.dma_start(wts[:, 0, :], w_u).then_inc(user_in, 16)
            act.wait_ge(eps_ok, 1)

            def pre_sd(g):
                act.wait_ge(var1_ok, g + 1)
                nc.scalar.activation(sd1[:, 0:PRE_GROUPS[g]], mv1[:, 0:PRE_GROUPS[g], 1], ACT.Sqrt,
                                     bias=eps[:, 0:1]).then_inc(sd1_ok, 1)

            def pre_copy(g):
                act.wait_ge(hT1_done, g + 1)
                for a in range(0, PRE_GROUPS[g], 4):
                    size = min(4, PRE_GROUPS[g] - a)
                    i = nc.scalar.copy(hT1[:, a:a + size, :],
                                       bank[4 + a // 4][0:d, 0:size * P].rearrange("p (t c) -> p t c", c=P))
                i.then_inc(hT1_ok, 1)

            def keep(k, s, b):
                act.wait_ge(tr_done, (k - BARE) * supers + s + 1)
                first, size = sum(CACHE_BLOCKS[:k]), CACHE_BLOCKS[k]
                src = tr_ps[b][:, 0:size * ROWS].rearrange("p (m u c) -> p m u c", m=size, u=SUB)
                dst = cache[:, first:first + size, bass.ds(s * ROWS, ROWS)].rearrange("p m (c u) -> p m u c", u=SUB)
                nc.scalar.copy(dst, src).then_inc(cache_ok, 1)

            def panel_end(k):
                act.wait_ge(used, (k + 1) * supers)
                gT = gT_first if k < PANELS - 1 else gT_last
                nb, nk = CHUNK_BLOCKS[k], CACHE_BLOCKS[k]
                for c in range(2):
                    half = acc1[HALF * c:HALF * (c + 1), :]
                    at = HALF * nk * c
                    groups = half[:, at:at + 2 * Q * nb].rearrange("p (g b q) -> p b g q", g=2, q=Q)
                    to = gT[HALF * c:HALF * (c + 1), :]
                    nc.scalar.copy(to[:, 0:2 * Q * nb].rearrange("p (b g q) -> p b g q", g=2, q=Q),
                                   groups).then_inc(gT_ok, 1)
                    if nk:
                        at = 2 * Q * nb * (1 - c)
                        kept = half[:, at:at + HALF * nk].rearrange("p (q m) -> p m q", m=nk)
                        nc.scalar.copy(to[:, 2 * Q * nb:].rearrange("p (m q) -> p m q", m=nk),
                                       kept).then_inc(gT_ok, 1)
                act.wait_ge(gb_done, k + 1)
                src = gb_ps[:, :].rearrange("p (b c) -> p b c", c=d)
                first, first_kept = sum(CHUNK_BLOCKS[:k]), sum(CACHE_BLOCKS[:k])
                nc.scalar.copy(g_sb[:, first:first + nb, :], src[:, 0:nb, :]).then_inc(g_ok, 1)
                if nk:
                    nc.scalar.copy(gc_sb[:, first_kept:first_kept + nk, :], src[:, nb:, :]).then_inc(g_ok, 1)

            pre_sd(0)
            pre_copy(0)
            pre_sd(1)
            act.dma_start(coef_i, diag_i.rearrange("(s p u) -> p s u", p=P, u=SUB)).then_inc(item_in, 16)
            act.dma_start(wts[:, 1, :], w_i).then_inc(item_in, 16)
            pre_copy(1)
            pre_sd(2)
            for g in range(n_pre):
                if g + 2 < n_pre:
                    pre_copy(g + 2)
                if g + 3 < n_pre:
                    pre_sd(g + 3)
            panel_end(0)
            for k in range(1, PANELS):
                if k == PANELS - 1:
                    act.wait_ge(y_step, 2 * n_pre)
                with act.Fori(0, (supers - PAIR_SLOTS) // 2, 1) as i:
                    keep(k, i * 2, 0)
                    keep(k, i * 2 + 1, 1)
                for s in range(supers - PAIR_SLOTS, supers):
                    keep(k, s, s % 2)
                    if k == PANELS - 1:
                        for m in range(CHUNKS):
                            if first_free(m) == pairs - supers + s + 1:
                                act.wait_ge(used, first_free(m))
                                pass2_load(act, 0, m, (2, 3))
                panel_end(k)

            def stage_rows(s):
                if not (isinstance(s, int) and s == 0):
                    act.wait_ge(stage_used, s)
                nc.scalar.copy(stage, cache[:, :, bass.ds(s * ROWS, ROWS)]).then_inc(stage_ok, 1)

            def superblock(s, b, first=False, load=True):
                def load_next(k):
                    if load:
                        act.wait_ge(used, uses(s, k))
                        pass2_load(act, s + 1, k, (2, 3))

                if not first:
                    act.wait_ge(used, uses(s - 1, CHUNKS - 1))
                    nc.scalar.copy(hT[:, 1 - b, :], acc2[1 - b]).then_inc(hT_ok, 1)
                load_next(0)
                if not first:
                    act.wait_ge(mv_ok, s * SUB)
                    nc.scalar.activation(sd[:], mv[:, :, 1], ACT.Sqrt, bias=eps[:, 0:1]).then_inc(sd_ok, 1)
                load_next(1)
                load_next(2)
                if load:
                    stage_rows(s + 1)
                load_next(3)
                load_next(4)

            act.wait_ge(cache_ok, (PANELS - BARE) * supers)
            stage_rows(0)
            superblock(0, 0, first=True)
            superblock(1, 1)
            with act.Fori(1, supers // 2 - 1, 1) as i:
                superblock(i * 2, 0)
                superblock(i * 2 + 1, 1)
            superblock(supers - 2, 0)
            superblock(supers - 1, 1, load=False)
            act.wait_ge(used, uses(supers - 1, CHUNKS - 1))
            nc.scalar.copy(hT[:, 1, :], acc2[1]).then_inc(hT_ok, 1)
            act.wait_ge(mv_ok, supers * SUB)
            nc.scalar.activation(sd[:], mv[:, :, 1], ACT.Sqrt, bias=eps[:, 0:1]).then_inc(sd_ok, 1)

        @block.vector
        def _(dve):
            steps = [0]

            def step(i):
                i.then_inc(step1, 1)
                steps[0] += 1

            def pre_norm(g):
                size = PRE_GROUPS[g]
                rows = x_sb[:, pre_at[g]:pre_at[g + 1], :]
                h = h_sb[:, g % 2, 0:size, :]
                dve.wait_ge(x_in[g], 16)
                for t in range(size):
                    step(nc.vector.bn_stats(st1[:, t, :], rows[:, t, :]))
                dve.wait_ge(step1, steps[0])
                for t in range(size):
                    step(nc.vector.bn_aggr(mv1[:, t, :], st1[:, t, :]))
                if g >= 2:
                    dve.wait_ge(y_step, 2 * (g - 2) + 1)
                dve.wait_ge(step1, steps[0])
                nc.vector.tensor_tensor(h, rows, mv1[:, 0:size, 0:1].broadcast_to([P, size, d]),
                                        ALU.subtract).then_inc(var1_ok, 1)
                dve.wait_ge(sd1_ok, g + 1)
                step(nc.vector.reciprocal(rs1[:, 0:size], sd1[:, 0:size]))
                dve.wait_ge(var1_ok, g + 1)
                dve.wait_ge(step1, steps[0])
                nc.vector.scalar_tensor_tensor(
                    out=h, in0=h, scalar=0.0, in1=rs1[:, 0:size].unsqueeze(2).broadcast_to([P, size, d]),
                    op0=ALU.max, op1=ALU.mult).then_inc(h_ok, 1)

            def pre_e(g):
                size = PRE_GROUPS[g]
                e = e_sb[:, pre_at[g]:pre_at[g + 1], :]
                dve.wait_ge(h_ok, g + 1)
                dve.wait_ge(hw_done, g + 1)
                c = coef[:, pre_at[g]:pre_at[g + 1]].unsqueeze(2).broadcast_to([P, size, d])
                step(nc.vector.tensor_tensor(e, e_ps[:, 0:size, :], c, ALU.mult))
                dve.wait_ge(step1, steps[0])
                nc.vector.tensor_tensor(e, e, h_sb[:, g % 2, 0:size, :], ALU.add).then_inc(e_ok, 1)

            pre_norm(0)
            dve.wait_ge(par_in, 16 * 2)
            nc.vector.tensor_tensor(parp, par[:, :, 0], par[:, :, 1], ALU.mult).then_inc(parp_ok, 1)
            dve.wait_ge(user_in, 16 * 2)
            dve.wait_ge(parp_ok, 1)
            nc.vector.tensor_scalar(coef[:, 0:user_tiles], coef[:, 0:user_tiles], parp[:, 0:1], None,
                                    ALU.mult).then_inc(coef_ok, 1)
            dve.wait_ge(coef_ok, 1)
            pre_e(0)
            for g in range(1, n_pre):
                pre_norm(g)
                if pre_at[g] == user_tiles:
                    dve.wait_ge(item_in, 16 * 2)
                    nc.vector.tensor_scalar(coef[:, user_tiles:tiles], coef[:, user_tiles:tiles], parp[:, 1:2],
                                            None, ALU.mult).then_inc(coef_ok, 1)
                    dve.wait_ge(coef_ok, 2)
                if g >= 2:
                    pre_e(g - 1)
            pre_e(n_pre - 1)

            def turn(s, k, parts=None):
                dve.wait_ge(loaded[k], (16 * PANELS * rounds if k < PAIR_SLOTS else 0) + 16 * GROUPS * (s + 1))
                if parts:
                    for a, b in parts:
                        cols = chunk(k)[:, :, Q * a:Q * b]
                        nc.vector.transpose(cols, cols).then_inc(turned, 1)
                else:
                    a = ring[:, chunk_at[k]:chunk_at[k] + chunk_size[k]]
                    nc.vector.transpose(a, a).then_inc(turned, 1)

            def stats(s, b):
                dve.wait_ge(ho_done, s + 1)
                for u in range(SUB):
                    nc.vector.bn_stats(st[:, u, :], ho_ps[b][:, u, :]).then_inc(st_ok, 1)
                dve.wait_ge(st_ok, SUB * (s + 1))

            def variances():
                for u in range(SUB):
                    nc.vector.bn_aggr(mv[:, u, :], st[:, u, :]).then_inc(mv_ok, 1)

            def scale(s, b, reused=True):
                if reused:
                    dve.wait_ge(stored[b], 8 * (s - b))
                dve.wait_ge(mv_ok, SUB * (s + 1))
                for u in range(SUB):
                    nc.vector.scalar_tensor_tensor(
                        out=o_sb[:, b, u, :], in0=ho_ps[b][:, u, :], scalar=mv[:, u, 0:1], in1=gam[:],
                        op0=ALU.subtract, op1=ALU.mult).then_inc(scaled_ok, 1)

            def finish(s, b):
                dve.wait_ge(sd_ok, s + 1)
                nc.vector.reciprocal(rs[:], sd[:]).then_inc(rs_ok, 1)
                dve.wait_ge(scaled_ok, SUB * (s + 1))
                dve.wait_ge(rs_ok, s + 1)
                for u in range(SUB):
                    o = o_sb[:, b, u, :]
                    y = x_sb[:, bass.ds(s * SUB + u, 1), :].rearrange("p t c -> p (t c)")
                    nc.vector.scalar_tensor_tensor(out=o, in0=o, scalar=rs[:, u:u + 1], in1=y,
                                                   op0=ALU.mult, op1=ALU.add).then_inc(o_ok, 1)

            def superblock(s, b, prev=True, reused=True, last=False):
                turn(s, 0)
                turn(s, 1)
                turn(s, 2)
                if prev:
                    stats(s - 1, 1 - b)
                turn(s, 3)
                if prev:
                    variances()
                    scale(s - 1, 1 - b, reused)
                    finish(s - 1, 1 - b)
                turn(s, 4, [(0, LAST_PART), (LAST_PART, CHUNK_BLOCKS[-1])] if last else None)

            superblock(0, 0, prev=False)
            superblock(1, 1, reused=False)
            superblock(2, 0, reused=False)
            superblock(3, 1)
            with dve.Fori(2, supers // 2 - 1, 1) as i:
                superblock(i * 2, 0)
                superblock(i * 2 + 1, 1)
            superblock(supers - 2, 0)
            superblock(supers - 1, 1, last=True)
            stats(supers - 1, 1)
            variances()
            scale(supers - 1, 1)
            finish(supers - 1, 1)

        @block.tensor
        def _(pe):
            def pre_transpose(g):
                pe.wait_ge(h_ok, g + 1)
                if g >= 1:
                    pe.wait_ge(hT1_ok, g)
                for t in range(PRE_GROUPS[g]):
                    i = nc.tensor.transpose(hT1_bank(t), h_sb[:, g % 2, t, :], ident[:])
                i.then_inc(hT1_done, 1)

            def pre_weights(g):
                if g == 0:
                    pe.wait_ge(user_in, 16 * 2)
                if pre_at[g] == user_tiles:
                    pe.wait_ge(item_in, 16 * 2)
                if g >= 1:
                    pe.wait_ge(e_ok, g)
                pe.wait_ge(hT1_ok, g + 1)
                w = wts[:, 0 if pre_at[g] < user_tiles else 1, :]
                for t in range(PRE_GROUPS[g]):
                    i = nc.tensor.matmul(e_ps[:, t, :], hT1[:, t, :], w, start=True, stop=True)
                i.then_inc(hw_done, 1)

            def pair(k, s, n_cached):
                slot = s % PAIR_SLOTS
                a = ring[:, slot * pair_size:(slot + 1) * pair_size].rearrange("p (u j) -> p u j", u=SUB)
                mid = (PANEL - n_cached * P) // 2
                if n_cached and s >= 2:
                    pe.wait_ge(cache_ok, (k - BARE) * supers + s - 1)
                pe.wait_ge(loaded[slot], 16 * (k * rounds + s // PAIR_SLOTS + 1))
                for m in range(n_cached):
                    for u in range(SUB):
                        at = m * ROWS + u * P
                        cols = a[:, u, mid:mid + n_cached * P].rearrange("p (c m) -> p m c", m=n_cached)[:, m, :]
                        i = nc.tensor.transpose(tr_ps[s % 2][:, at:at + P], cols, ident[:])
                if n_cached:
                    i.then_inc(tr_done, 1)
                for u in range(SUB):
                    t = s * SUB + u
                    for c in range(2):
                        i = nc.tensor.matmul(acc1[HALF * c:HALF * (c + 1), :], e_sb[:, t, :],
                                             a[:, u, c * (PANEL // 2):(c + 1) * (PANEL // 2)],
                                             start=(t == 0), stop=(t == tiles - 1))
                i.then_inc(used, 1)

            def turn_back(gT):
                for b in range(PANEL_BLOCKS):
                    for c in range(2):
                        rows = slice(HALF * c, HALF * (c + 1))
                        i = nc.tensor.matmul(gb_ps[rows, b * d:(b + 1) * d], gT[rows, HALF * b:HALF * (b + 1)],
                                             ident2[rows, :], start=True, stop=True)
                i.then_inc(gb_done, 1)

            pe.wait_ge(ident_ok, 1)
            pre_transpose(0)
            pre_weights(0)
            for g in range(n_pre):
                pe.wait_ge(e_ok, g + 1)
                first, end = pre_at[g] // SUB, pre_at[g + 1] // SUB
                pair(0, first, CACHE_BLOCKS[0])
                if g == 0:
                    pre_transpose(1)
                if g + 1 < n_pre:
                    pre_weights(g + 1)
                for s in range(first + 1, end):
                    pair(0, s, CACHE_BLOCKS[0])
                if g + 2 < n_pre:
                    pre_transpose(g + 2)
            pe.wait_ge(ident2_ok, 1)

            def panel(k, n_cached):
                pe.wait_ge(gT_ok, 4 * k - 2 * BARE)
                pair(k, 0, n_cached)
                turn_back(gT_first)
                for s in range(1, supers):
                    pair(k, s, n_cached)

            for n_cached in sorted(set(CACHE_BLOCKS[BARE:])):
                first = CACHE_BLOCKS.index(n_cached)
                with pe.Fori(first, CACHE_BLOCKS.index(n_cached) + CACHE_BLOCKS.count(n_cached), 1) as k:
                    panel(k, n_cached)

            def multiply(s, b, k):
                pe.wait_ge(turned, s * CHUNKS + k + 1)
                a = chunk(k)
                for m in range(CHUNK_BLOCKS[k]):
                    if isinstance(s, int) and s == supers - 1 and k == CHUNKS - 1 and m == LAST_PART:
                        pe.wait_ge(turned, supers * CHUNKS + 1)
                    blk = sum(CHUNK_BLOCKS[:k]) + m
                    c = (cached + blk) % 2
                    i = nc.tensor.matmul(acc2[b][HALF * c:HALF * (c + 1), :], g_sb[:, blk, :],
                                         a[:, :, Q * m:Q * (m + 1)], start=(isinstance(s, int) and s == 0 and blk < 2),
                                         stop=(blk >= blocks - 2))
                i.then_inc(used, 1)
                return i

            def multiply_cached(s, b):
                pe.wait_ge(stage_ok, s + 1)
                for m in range(cached):
                    c = m % 2
                    i = nc.tensor.matmul(acc2[b][HALF * c:HALF * (c + 1), :], gc_sb[:, m, :], stage[:, m, :],
                                         start=(not (isinstance(s, int) and s == 0) and m < 2), stop=False)
                i.then_inc(stage_used, 1)

            def rows_out(s, b):
                pe.wait_ge(hT_ok, s + 1)
                if not (isinstance(s, int) and s < 2):
                    pe.wait_ge(scaled_ok, SUB * (s - 1))
                for u in range(SUB):
                    cols = hT[:, b, :].rearrange("p (c u) -> p u c", u=SUB)[:, u, :]
                    i = nc.tensor.matmul(ho_ps[b][:, u, :], cols, ident2[:], start=True, stop=True)
                i.then_inc(ho_done, 1)

            def superblock(s, b):
                multiply_cached(s, b)
                multiply(s, b, 0)
                rows_out(s - 1, 1 - b)
                for k in range(1, CHUNKS):
                    multiply(s, b, k)

            multiply(0, 0, 0)
            pe.wait_ge(gT_ok, 4 * PANELS - 2 * BARE)
            turn_back(gT_last)
            multiply(0, 0, 1)
            multiply(0, 0, 2)
            pe.wait_ge(g_ok, 2 * PANELS - BARE)
            multiply_cached(0, 0)
            multiply(0, 0, 3)
            multiply(0, 0, 4)
            superblock(1, 1)
            superblock(2, 0)
            superblock(3, 1)
            with pe.Fori(2, supers // 2 - 1, 1) as i:
                superblock(i * 2, 0)
                superblock(i * 2 + 1, 1)
            superblock(supers - 2, 0)
            superblock(supers - 1, 1)
            rows_out(supers - 1, 1)


_INS = ["x", "adj", "L0_gnn_W_u", "L0_gnn_diag_u", "L0_gnn_par_u", "L0_gnn_W_i", "L0_gnn_diag_i",
        "L0_gnn_par_i", "L0_gnn_ln_gamma", "L0_gnn_ln_beta"]


def kernel(**inputs):
    import numpy as _np
    import concourse.bacc as _bacc
    from concourse.bass_utils import run_bass_kernel_spmd as _run

    nc = _bacc.Bacc("TRN2", target_bir_lowering=False, num_devices=1)
    arrays, args = {}, []
    for name in _INS:
        a = _np.ascontiguousarray(inputs[name])
        arrays[f"in_{name}"] = a
        args.append(nc.dram_tensor(f"in_{name}", a.shape, mybir.dt.from_np(a.dtype), kind="ExternalInput").ap())
    result = nc.dram_tensor("result", arrays["in_x"].shape, F32, kind="ExternalOutput").ap()
    gnn_kernel(nc, *args, result)
    r = _run(nc, [arrays], core_ids=[0])
    return r.results[0]["result"]
```
